# Optimizing a Trainium2 kernel written in Bass

```python
import numpy as np
import jax
import jax.numpy as jnp

def _softmax(x, axis=-1):
    return jax.nn.softmax(x, axis=axis)

def _gelu(x):
    return jax.nn.gelu(x, approximate=True)

def _silu(x):
    return jax.nn.silu(x)

def _sigmoid(x):
    return jax.nn.sigmoid(x)

def _layernorm(x, axis=-1, eps=1e-05):
    m = jnp.mean(x, axis=axis, keepdims=True)
    v = jnp.var(x, axis=axis, keepdims=True)
    return (x - m) / jnp.sqrt(v + eps)

def _scatter_add(tgt, idx, src, axis=0):
    return tgt.at[idx].add(src)

def _segment_sum(src, seg, n):
    return jax.ops.segment_sum(src, seg, n)
kernel_name = 'mk_seq_preln_d1_jaxref_r2_b5c8cb'

def setup_inputs(seed: int=0):
    np.random.seed(seed)
    _w = jnp.asarray

    def _L0_attn_setup():
        import jax, jax.numpy as jnp
        import numpy as np
        B, L, D, N, K, E = (8, 2048, 512, 16, 4, 2)
        INNER = E * N

        def _selective_ssm(x, conv_w, conv_b, Win, b_in, Wout, b_out, A_log):
            bsz, seq_len, d_model = x.shape
            n = A_log.shape[0]
            inner = (Win.shape[1] - n) // 2
            pad = (conv_w.shape[2] - 1) // 2
            xc = jnp.transpose(x, (0, 2, 1))
            xc = jax.lax.conv_general_dilated(xc, conv_w, window_strides=(1,), padding=[(pad, pad)], dimension_numbers=('NCH', 'OIH', 'NCH'), feature_group_count=d_model)
            xc = xc + conv_b[None, :, None]
            Lc = xc.shape[2]
            if Lc < seq_len:
                xc = jnp.pad(xc, ((0, 0), (0, 0), (0, seq_len - Lc)))
            elif Lc > seq_len:
                xc = xc[:, :, :seq_len]
            xc = jnp.transpose(xc, (0, 2, 1))
            proj = xc @ Win + b_in
            delta = proj[..., :n]
            B_in = proj[..., n:n + inner].reshape(bsz, seq_len, n, -1).mean(axis=-1)
            C = proj[..., n + inner:].reshape(bsz, seq_len, n, -1).mean(axis=-1)
            A = -jnp.exp(A_log)[None, None, :]
            dA = jax.nn.softplus(delta) * A
            A_bar = jnp.exp(dA)
            eps = 0.0001
            A_safe = jnp.where(jnp.abs(A) < eps, eps * jnp.sign(A) + eps, A)
            taylor = 1.0 + dA / 2.0 + dA * dA / 6.0
            B_bar_scale = jnp.where(jnp.abs(A) < eps, taylor, (A_bar - 1.0) / A_safe)
            B_bar = B_bar_scale * B_in

            def combine(c1, c2):
                a1, b1 = c1
                a2, b2 = c2
                return (a1 * a2, a2 * b1 + b2)
            _, h = jax.lax.associative_scan(combine, (A_bar, B_bar), axis=1)
            y = C * h @ Wout + b_out
            return y
        key = jax.random.key(seed)
        ks = jax.random.split(key, 4)
        x = jax.random.normal(ks[0], (B, L, D), jnp.float32)
        conv_w = jax.random.normal(ks[1], (D, 1, K), jnp.float32) * (1.0 / np.sqrt(K))
        conv_b = jnp.zeros((D,), jnp.float32)
        Win = jax.random.normal(ks[2], (D, 2 * INNER + N), jnp.float32) * (1.0 / np.sqrt(D))
        b_in = jnp.zeros((2 * INNER + N,), jnp.float32)
        Wout = jax.random.normal(ks[3], (N, D), jnp.float32) * (1.0 / np.sqrt(N))
        b_out = jnp.zeros((D,), jnp.float32)
        A_log = jnp.zeros((N,), jnp.float32)
        return {'x': x, 'conv_w': conv_w, 'conv_b': conv_b, 'Win': Win, 'b_in': b_in, 'Wout': Wout, 'b_out': b_out, 'A_log': A_log}
    _L0_attn_in = _L0_attn_setup()

    def _L0_ffn_setup():
        import jax, jax.numpy as jnp
        import numpy as np
        N_GROUP = 8
        TOPK_GROUP = 4
        TOPK = 8
        ROUTED_SCALE = 2.5
        B, S, D, F, E = (4, 1024, 512, 256, 64)

        def _route(x, w_router, b_router):
            scores = jax.nn.sigmoid(jnp.einsum('bsd,de->bse', x, w_router)).astype(jnp.float32)
            swb = scores + b_router
            e = scores.shape[-1]
            group_scores = jnp.sum(jax.lax.top_k(swb.reshape(swb.shape[:-1] + (N_GROUP, -1)), 2)[0], axis=-1)
            group_idx = jax.lax.top_k(group_scores, TOPK_GROUP)[1]
            mask = jnp.any(jnp.arange(N_GROUP)[:, None] == group_idx[..., None, :], axis=-1)
            mask = jnp.repeat(mask, e // N_GROUP, axis=-1)
            masked_scores = jnp.where(mask, swb, 0.0)
            topk_idx = jax.lax.top_k(masked_scores, TOPK)[1]
            topk_w = jnp.take_along_axis(scores, topk_idx, axis=-1).astype(jnp.float32)
            topk_w = ROUTED_SCALE * topk_w / (jnp.sum(topk_w, axis=-1)[..., None] + 1e-20)
            return (topk_w, topk_idx)

        def _moe_forward(x, w_router, b_router, we_gate, we_up, we_down, ws_gate, ws_up, ws_down):
            b, s, d = x.shape
            e = we_gate.shape[0]
            topk_w, topk_idx = _route(x, w_router, b_router)
            x_flat = x.reshape(-1, d)
            idx_flat = topk_idx.reshape(-1)
            sort = jnp.argsort(idx_flat)
            tok = sort // TOPK
            x_sorted = x_flat[tok]
            group_sizes = jnp.bincount(idx_flat, length=e).astype(jnp.int32)
            g = jax.lax.ragged_dot(x_sorted, we_gate, group_sizes)
            u = jax.lax.ragged_dot(x_sorted, we_up, group_sizes)
            o = jax.lax.ragged_dot(jax.nn.silu(g) * u, we_down, group_sizes)
            w_sorted = topk_w.reshape(-1)[sort].astype(o.dtype)
            y = jnp.zeros_like(x_flat).at[tok].add(o * w_sorted[:, None])
            y = y.reshape(b, s, d)
            shared = jnp.einsum('btf,fd->btd', jax.nn.silu(jnp.einsum('btd,df->btf', x, ws_gate)) * jnp.einsum('btd,df->btf', x, ws_up), ws_down)
            return y + shared
        key = jax.random.key(seed)
        ks = jax.random.split(key, 10)
        sd = 1.0 / np.sqrt(D)
        sf = 1.0 / np.sqrt(F)
        return {'x': jax.random.normal(ks[0], (B, S, D), jnp.float32), 'w_router': jax.random.normal(ks[1], (D, E), jnp.float32) * sd, 'b_router': jax.random.normal(ks[2], (E,), jnp.float32) * 0.1, 'we_gate': jax.random.normal(ks[3], (E, D, F), jnp.float32) * sd, 'we_up': jax.random.normal(ks[4], (E, D, F), jnp.float32) * sd, 'we_down': jax.random.normal(ks[5], (E, F, D), jnp.float32) * sf, 'ws_gate': jax.random.normal(ks[6], (D, F), jnp.float32) * sd, 'ws_up': jax.random.normal(ks[7], (D, F), jnp.float32) * sd, 'ws_down': jax.random.normal(ks[8], (F, D), jnp.float32) * sf}
    _L0_ffn_in = _L0_ffn_setup()
    _d = {'L0_attn_x': _L0_attn_in['x'], 'L0_attn_conv_w': _L0_attn_in['conv_w'], 'L0_attn_conv_b': _L0_attn_in['conv_b'], 'L0_attn_Win': _L0_attn_in['Win'], 'L0_attn_b_in': _L0_attn_in['b_in'], 'L0_attn_Wout': _L0_attn_in['Wout'], 'L0_attn_b_out': _L0_attn_in['b_out'], 'L0_attn_A_log': _L0_attn_in['A_log'], 'L0_ffn_w_router': _L0_ffn_in['w_router'], 'L0_ffn_b_router': _L0_ffn_in['b_router'], 'L0_ffn_we_gate': _L0_ffn_in['we_gate'], 'L0_ffn_we_up': _L0_ffn_in['we_up'], 'L0_ffn_we_down': _L0_ffn_in['we_down'], 'L0_ffn_ws_gate': _L0_ffn_in['ws_gate'], 'L0_ffn_ws_up': _L0_ffn_in['ws_up'], 'L0_ffn_ws_down': _L0_ffn_in['ws_down']}
    _x0 = _d['L0_attn_x']
    _d['L0_attn_x'] = jax.random.normal(jax.random.fold_in(jax.random.key(seed), 1), (4, 2048, 512), dtype=_x0.dtype)
    del _x0
    return _d

def reference(L0_attn_x, L0_attn_conv_w, L0_attn_conv_b, L0_attn_Win, L0_attn_b_in, L0_attn_Wout, L0_attn_b_out, L0_attn_A_log, L0_ffn_w_router, L0_ffn_b_router, L0_ffn_we_gate, L0_ffn_we_up, L0_ffn_we_down, L0_ffn_ws_gate, L0_ffn_ws_up, L0_ffn_ws_down):

    def _L0_attn_ref(x, conv_w, conv_b, Win, b_in, Wout, b_out, A_log):
        import jax, jax.numpy as jnp
        import numpy as np
        B, L, D, N, K, E = (8, 2048, 512, 16, 4, 2)
        INNER = E * N

        def _selective_ssm(x, conv_w, conv_b, Win, b_in, Wout, b_out, A_log):
            bsz, seq_len, d_model = x.shape
            n = A_log.shape[0]
            inner = (Win.shape[1] - n) // 2
            pad = (conv_w.shape[2] - 1) // 2
            xc = jnp.transpose(x, (0, 2, 1))
            xc = jax.lax.conv_general_dilated(xc, conv_w, window_strides=(1,), padding=[(pad, pad)], dimension_numbers=('NCH', 'OIH', 'NCH'), feature_group_count=d_model)
            xc = xc + conv_b[None, :, None]
            Lc = xc.shape[2]
            if Lc < seq_len:
                xc = jnp.pad(xc, ((0, 0), (0, 0), (0, seq_len - Lc)))
            elif Lc > seq_len:
                xc = xc[:, :, :seq_len]
            xc = jnp.transpose(xc, (0, 2, 1))
            proj = xc @ Win + b_in
            delta = proj[..., :n]
            B_in = proj[..., n:n + inner].reshape(bsz, seq_len, n, -1).mean(axis=-1)
            C = proj[..., n + inner:].reshape(bsz, seq_len, n, -1).mean(axis=-1)
            A = -jnp.exp(A_log)[None, None, :]
            dA = jax.nn.softplus(delta) * A
            A_bar = jnp.exp(dA)
            eps = 0.0001
            A_safe = jnp.where(jnp.abs(A) < eps, eps * jnp.sign(A) + eps, A)
            taylor = 1.0 + dA / 2.0 + dA * dA / 6.0
            B_bar_scale = jnp.where(jnp.abs(A) < eps, taylor, (A_bar - 1.0) / A_safe)
            B_bar = B_bar_scale * B_in

            def combine(c1, c2):
                a1, b1 = c1
                a2, b2 = c2
                return (a1 * a2, a2 * b1 + b2)
            _, h = jax.lax.associative_scan(combine, (A_bar, B_bar), axis=1)
            y = C * h @ Wout + b_out
            return y
        return _selective_ssm(x, conv_w, conv_b, Win, b_in, Wout, b_out, A_log)

    def _L0_ffn_ref(x, w_router, b_router, we_gate, we_up, we_down, ws_gate, ws_up, ws_down):
        import jax, jax.numpy as jnp
        import numpy as np
        N_GROUP = 8
        TOPK_GROUP = 4
        TOPK = 8
        ROUTED_SCALE = 2.5
        B, S, D, F, E = (4, 1024, 512, 256, 64)

        def _route(x, w_router, b_router):
            scores = jax.nn.sigmoid(jnp.einsum('bsd,de->bse', x, w_router)).astype(jnp.float32)
            swb = scores + b_router
            e = scores.shape[-1]
            group_scores = jnp.sum(jax.lax.top_k(swb.reshape(swb.shape[:-1] + (N_GROUP, -1)), 2)[0], axis=-1)
            group_idx = jax.lax.top_k(group_scores, TOPK_GROUP)[1]
            mask = jnp.any(jnp.arange(N_GROUP)[:, None] == group_idx[..., None, :], axis=-1)
            mask = jnp.repeat(mask, e // N_GROUP, axis=-1)
            masked_scores = jnp.where(mask, swb, 0.0)
            topk_idx = jax.lax.top_k(masked_scores, TOPK)[1]
            topk_w = jnp.take_along_axis(scores, topk_idx, axis=-1).astype(jnp.float32)
            topk_w = ROUTED_SCALE * topk_w / (jnp.sum(topk_w, axis=-1)[..., None] + 1e-20)
            return (topk_w, topk_idx)

        def _moe_forward(x, w_router, b_router, we_gate, we_up, we_down, ws_gate, ws_up, ws_down):
            b, s, d = x.shape
            e = we_gate.shape[0]
            topk_w, topk_idx = _route(x, w_router, b_router)
            x_flat = x.reshape(-1, d)
            idx_flat = topk_idx.reshape(-1)
            sort = jnp.argsort(idx_flat)
            tok = sort // TOPK
            x_sorted = x_flat[tok]
            group_sizes = jnp.bincount(idx_flat, length=e).astype(jnp.int32)
            g = jax.lax.ragged_dot(x_sorted, we_gate, group_sizes)
            u = jax.lax.ragged_dot(x_sorted, we_up, group_sizes)
            o = jax.lax.ragged_dot(jax.nn.silu(g) * u, we_down, group_sizes)
            w_sorted = topk_w.reshape(-1)[sort].astype(o.dtype)
            y = jnp.zeros_like(x_flat).at[tok].add(o * w_sorted[:, None])
            y = y.reshape(b, s, d)
            shared = jnp.einsum('btf,fd->btd', jax.nn.silu(jnp.einsum('btd,df->btf', x, ws_gate)) * jnp.einsum('btd,df->btf', x, ws_up), ws_down)
            return y + shared
        return _moe_forward(x, w_router, b_router, we_gate, we_up, we_down, ws_gate, ws_up, ws_down)
    x = L0_attn_x
    x = x + _L0_attn_ref(_layernorm(x, axis=-1), L0_attn_conv_w, L0_attn_conv_b, L0_attn_Win, L0_attn_b_in, L0_attn_Wout, L0_attn_b_out, L0_attn_A_log)
    x = x + _L0_ffn_ref(_layernorm(x, axis=-1), L0_ffn_w_router, L0_ffn_b_router, L0_ffn_we_gate, L0_ffn_we_up, L0_ffn_we_down, L0_ffn_ws_gate, L0_ffn_ws_up, L0_ffn_ws_down)
    return x

_drawn_inputs = setup_inputs


def setup_inputs(seed=0):
    import zlib

    import numpy as np

    out = dict(_drawn_inputs(seed))
    spreads = {'L0_attn_conv_b': (0.0, 0.1),
     'L0_attn_b_in': (0.0, 0.1),
     'L0_attn_b_out': (0.0, 0.1),
     'L0_attn_A_log': (0.0, 0.1)}
    factors = {}
    for name, (base, spread) in spreads.items():
        noise = np.random.default_rng([zlib.crc32(name.encode()), seed]).standard_normal(out[name].shape)
        drawn = base * np.exp(spread * noise) if base else spread * noise
        out[name] = jnp.asarray(drawn.astype(out[name].dtype))
    for name, factor in factors.items():
        out[name] = (out[name] * factor).astype(out[name].dtype)
    return out
```

```python
from contextlib import ExitStack

import concourse.bass as bass
from concourse import mybir

ALU = mybir.AluOpType
ACT = mybir.ActivationFunctionType
AX = mybir.AxisListType
F32 = mybir.dt.float32
F32R = mybir.dt.float32r
BF16 = mybir.dt.bfloat16
I32 = mybir.dt.int32
U32 = mybir.dt.uint32

P = 128
B, L, D = 4, 2048, 512
T = B * L
DC = D // P
N_STATE, TAPS = 16, 4
PROJ = 3 * N_STATE
E, F, TOPK = 64, 256, 8
FC = F // P
GROUPS, TOP_GROUPS = 8, 4
GSIZE = E // GROUPS
ROUTED_SCALE = 2.5
LN_EPS = 1e-5
A_EPS = 1e-4
ROW = D + E
REGION = T
SLOT0 = P
SLOTS = 66 * REGION
TILES = T * TOPK // P + E
SUB = 4
WSLOTS = 4
UNROLL = 8
NEG = -3.0e38


class Shared:
    pass


def after(eng, sem, count):
    if not isinstance(count, int) or count > 0:
        eng.wait_ge(sem, count)


def peeled(eng, n, body):
    body(0)
    with eng.Fori(1, n - 1) as i:
        body(i)
    body(n - 1)


def constants(nc, k):
    with ExitStack() as ctx:
        fill = ctx.enter_context(nc.sbuf_tensor("fill", [P, SLOTS // P], I32))
        zeros = ctx.enter_context(nc.sbuf_tensor("zeros", [P, ROW], F32))
        made = ctx.enter_context(nc.semaphore("consts_made"))
        cleared = ctx.enter_context(nc.semaphore("consts_cleared"))
        dve_made = ctx.enter_context(nc.semaphore("consts_dve_made"))
        loaded = ctx.enter_context(nc.semaphore("consts_loaded"))
        stored = ctx.enter_context(nc.semaphore("consts_stored"))
        block = ctx.enter_context(nc.Block())

        @block.gpsimd
        def _(pool):
            nc.gpsimd.memset(k.ident[:], 0.0).then_inc(cleared, 1)
            nc.gpsimd.memset(k.tri[:], 1.0).then_inc(cleared, 1)
            nc.gpsimd.memset(k.ones[:], 1.0)
            nc.gpsimd.memset(k.nhalf[:], -0.5)
            nc.gpsimd.memset(k.euler[:], 2.718281828459045)
            nc.gpsimd.iota(fill[:].rearrange("p (r c) -> p r c", c=P), [[0, SLOTS // P // P], [1, P]],
                           base=T, channel_multiplier=0).then_inc(made, 1)
            nc.gpsimd.iota(k.slot_base_i[:], [[REGION, E]], base=SLOT0, channel_multiplier=0).then_inc(made, 1)
            nc.gpsimd.iota(k.token_i[:], [[L, SUB]], base=0, channel_multiplier=1).then_inc(made, 1)
            nc.gpsimd.iota(k.tile_i[:], [[P, TILES // P + 1]], base=0, channel_multiplier=1).then_inc(made, 1)
            pool.wait_ge(cleared, 2)
            nc.gpsimd.affine_select(out=k.ident[:], in_=k.ident[:], compare_op=ALU.not_equal, fill=1.0,
                                    base=0, pattern=[[-1, P]], channel_multiplier=1).then_inc(made, 1)
            nc.gpsimd.affine_select(out=k.tri[:], in_=k.tri[:], compare_op=ALU.is_gt, fill=0.0,
                                    base=0, pattern=[[1, P]], channel_multiplier=-1).then_inc(made, 1)

        @block.vector
        def _(dve):
            nc.vector.memset(zeros[:], 0.0).then_inc(dve_made, 1)
            nc.vector.memset(k.wout[:], 0.0).then_inc(dve_made, 1)
            dve.wait_ge(made, 4)
            nc.vector.tensor_copy(k.slot_base[:], k.slot_base_i[:])
            nc.vector.tensor_copy(k.slot_next[:], k.slot_base_i[:])
            nc.vector.tensor_copy(k.token_f[:], k.token_i[:])
            nc.vector.tensor_copy(k.tile_f[:], k.tile_i[:])

        @block.sync
        def _(sp):
            sp.wait_ge(dve_made, 2)
            for b in range(B):
                sp.dma_start(k.wout[N_STATE * b:N_STATE * (b + 1), b, :], k.Wout).then_inc(loaded, 16)
                sp.dma_start(k.wout[B * N_STATE:B * N_STATE + 1, b, :], k.b_out.unsqueeze(0)).then_inc(loaded, 16)
            sp.dma_start(k.router_bias[:], k.b_router.partition_broadcast(P)).then_inc(loaded, 16)
            sp.dma_start(k.rows[T:T + P, :], zeros[:]).then_inc(stored, 16)
            sp.dma_start(k.out[T:T + P, :], zeros[:, 0:D]).then_inc(stored, 16)
            sp.wait_ge(made, 1)
            sp.dma_start(k.slots.rearrange("(p c) o -> p (c o)", p=P), fill[:].bitcast(U32)).then_inc(stored, 16)
            sp.wait_ge(loaded, 16 * (2 * B + 1))
            sp.wait_ge(stored, 48)


def ssm_inputs(nc, k):
    QT = 4
    QL = L // QT
    HB = 64
    with ExitStack() as ctx:
        def sb(name, shape, dt=F32):
            return ctx.enter_context(nc.sbuf_tensor(name, shape, dt))

        def ps(name, shape, dt=F32):
            return ctx.enter_context(nc.psum_tensor(name, shape, dt))

        def sem(name):
            return ctx.enter_context(nc.semaphore("a_" + name))

        x_in = sb("a_x", [P, SUB, D])
        stats = sb("a_stats", [P, SUB, 6])
        moments = sb("a_moments", [P, SUB, 2])
        var_eps = sb("a_var_eps", [P, SUB])
        rstd = sb("a_rstd", [P, SUB])
        xn = sb("a_xn", [P, SUB, D])
        xnT = sb("a_xnT", [P, DC, L + 2])
        win = sb("a_win", [P, DC, N_STATE * 5])
        win48 = sb("a_win48", [P, DC, PROJ])
        taps = sb("a_taps", [P, DC, TAPS])
        conv_b = sb("a_conv_b", [P, DC])
        wtap = sb("a_wtap", [P, 2, DC, P])
        b_pair = sb("a_b_pair", [PROJ, 2])
        b48 = sb("a_b48", [PROJ, 1])
        bias = sb("a_bias", [P, 1])
        proj = sb("a_proj", [P, L + 1])
        turned = [ps(f"a_turned{i}", [P, DC, P]) for i in range(4)]
        product = [ps(f"a_product{i}", [P, QL]) for i in range(2)]
        bias_ps = ps("a_bias_ps", [P, 1])

        w_loaded = sem("w_loaded")
        x_loaded = [sem(f"x_loaded{i}") for i in range(SUB)]
        dve = sem("dve")
        w_ready = sem("w_ready")
        b48_made = sem("b48_made")
        bias_summed = sem("bias_summed")
        bias_ready = sem("bias_ready")
        edges = sem("edges")
        stats_done = sem("stats_done")
        var_ready = sem("var_ready")
        rstd_ready = sem("rstd_ready")
        normed = sem("normed")
        turned_done = sem("turned_done")
        xnT_ready = sem("xnT_ready")
        product_done = sem("product_done")
        proj_ready = sem("proj_ready")
        last_set = sem("last_set")
        proj_stored = sem("proj_stored")
        block = ctx.enter_context(nc.Block())
        NT = L // P

        @block.sync
        def _(sp):
            sp.dma_start(win[:], k.Win.rearrange("(c p) n -> p c n", p=P)).then_inc(w_loaded, 16)
            sp.dma_start(taps[:], k.conv_w.rearrange("(c p) o t -> p c (o t)", p=P)).then_inc(w_loaded, 16)
            with nc.allow_non_contiguous_dma(reason="512 biases"):
                sp.dma_start(conv_b[:], k.conv_b.rearrange("(c p) -> p c", p=P)).then_inc(w_loaded, 16)
            for j in range(2):
                sp.dma_start(b_pair[0:N_STATE, j:j + 1], k.b_in[0:N_STATE].unsqueeze(1)).then_inc(w_loaded, 16)
            sp.dma_start(b_pair[N_STATE:PROJ, :], k.b_in[N_STATE:5 * N_STATE].rearrange("(n j) -> n j", j=2)) \
                .then_inc(w_loaded, 16)

            def batch(b):
                for q in range(QT):
                    for s in range(SUB):
                        sp.wait_ge(normed, NT * b + SUB * q + s + 1)
                        sp.dma_start(x_in[:, s, :], k.x_blocks[b, SUB * q + s]).then_inc(x_loaded[s], 16)

            peeled(sp, B, batch)
            sp.wait_ge(proj_stored, 32 * B)

        @block.gpsimd
        def _(pool):
            def quarter(n):
                pool.wait_ge(var_ready, n + 1)
                nc.gpsimd.tensor_tensor(rstd[:], var_eps[:], k.nhalf[:], ALU.pow).then_inc(rstd_ready, 1)
            with pool.Fori(0, B * QT) as n:
                quarter(n)

        @block.vector
        def _(v):
            v.sem_inc(normed, SUB)
            nc.vector.memset(xnT[:, :, 0:1], 0.0).then_inc(edges, 1)
            nc.vector.memset(xnT[:, :, L + 1:L + 2], 0.0).then_inc(edges, 1)
            nc.vector.memset(proj[HB:P, L:L + 1], 0.0).then_inc(edges, 1)
            nc.vector.memset(wtap[:], 0.0)
            nc.vector.memset(bias[:], 0.0)
            v.wait_ge(w_loaded, 16 * 6)
            nc.vector.tensor_copy(win48[:, :, 0:N_STATE], win[:, :, 0:N_STATE])
            pairs = win[:, :, N_STATE:].rearrange("p c (n j) -> p c n j", j=2)
            nc.vector.tensor_tensor(win48[:, :, N_STATE:], pairs[:, :, :, 0], pairs[:, :, :, 1], ALU.add)
            nc.vector.tensor_tensor(b48[:], b_pair[:, 0:1], b_pair[:, 1:2], ALU.add)
            v.drain()
            nc.vector.tensor_scalar(win48[:, :, N_STATE:], win48[:, :, N_STATE:], 0.5, None, ALU.mult)
            nc.vector.tensor_scalar(b48[:], b48[:], 0.5, None, ALU.mult).then_inc(b48_made, 1)
            v.drain()
            for pair in range(2):
                for c in range(DC):
                    for half in range(2):
                        t = 2 * pair + half
                        nc.vector.tensor_scalar(wtap[:, pair, c, HB * half:HB * half + PROJ], win48[:, c, :],
                                                taps[:, c, t:t + 1], None, ALU.mult)
            v.drain().then_inc(w_ready, 1)
            v.wait_ge(bias_summed, 1)
            nc.vector.tensor_tensor(bias[0:PROJ, :], bias_ps[0:PROJ, :], b48[:], ALU.add).then_inc(bias_ready, 1)

            with v.Fori(0, B * QT) as n:
                for s in range(SUB):
                    v.wait_ge(x_loaded[s], 16 * n + 16)
                    nc.vector.bn_stats(stats[:, s, :], x_in[:, s, :])
                v.drain()
                for s in range(SUB):
                    nc.vector.bn_aggr(moments[:, s, :], stats[:, s, :])
                v.drain()
                nc.vector.tensor_scalar(var_eps[:], moments[:, :, 1], LN_EPS, None, ALU.add).then_inc(var_ready, 1)
                v.wait_ge(rstd_ready, n + 1)
                for s in range(SUB):
                    v.wait_ge(turned_done, SUB * n + s + 1)
                    nc.vector.tensor_scalar(xn[:, s, :], x_in[:, s, :], moments[:, s, 0:1], rstd[:, s:s + 1],
                                            ALU.subtract, ALU.mult).then_inc(normed, 1)

        @block.tensor
        def _(pe):
            pe.sem_inc(turned_done, SUB)
            pe.sem_inc(product_done, QT)
            pe.wait_ge(w_ready, 1)
            for c in range(DC):
                last = nc.tensor.matmul(bias_ps[0:PROJ, :], win48[:, c, :], conv_b[:, c:c + 1],
                                        start=(c == 0), stop=(c == DC - 1))
            last.then_inc(bias_summed, 1)

            def turn(b, q):
                for s in range(SUB):
                    i = NT * b + SUB * q + s
                    pe.wait_ge(normed, i + 1 + SUB)
                    pe.wait_ge(xnT_ready, i + 1)
                    for c in range(DC):
                        last = nc.tensor.transpose(turned[s][:, c, :], xn[:, s, c * P:(c + 1) * P], k.ident[:])
                    last.then_inc(turned_done, 1)

            def project(b, q):
                pe.wait_ge(xnT_ready, NT * b + min(SUB * (q + 1) + 1, NT) + SUB)
                pe.wait_ge(proj_ready, QT * b + q + 1)
                for pair in range(2):
                    for c in range(DC):
                        at = QL * q + 2 * pair
                        last = nc.tensor.matmul(product[q % 2][:], wtap[:, pair, c, :], xnT[:, c, at:at + QL],
                                                start=(pair == 0 and c == 0), stop=(pair == 1 and c == DC - 1))
                last.then_inc(product_done, 1)

            with pe.Fori(0, B) as b:
                turn(b, 0)
                for q in range(1, QT):
                    turn(b, q)
                    project(b, q - 1)
                project(b, QT - 1)

        @block.scalar
        def _(act):
            act.sem_inc(xnT_ready, SUB)
            act.sem_inc(proj_ready, 2)
            act.wait_ge(bias_ready, 1)
            act.wait_ge(b48_made, 1)
            act.wait_ge(edges, 3)

            def keep_turned(b, q):
                act.wait_ge(product_done, QT * b + min(q + 2, QT))
                for s in range(SUB):
                    i = NT * b + SUB * q + s
                    act.wait_ge(turned_done, i + 1 + SUB)
                    at = 1 + P * (SUB * q + s)
                    nc.scalar.activation(xnT[:, :, at:at + P], turned[s][:], ACT.Identity).then_inc(xnT_ready, 1)

            def keep_product(b, q):
                act.wait_ge(product_done, QT * b + q + 1 + QT)
                if q == 0:
                    after(act, proj_stored, 32 * b)
                nc.scalar.activation(proj[:, QL * q:QL * (q + 1)], product[q % 2][:], ACT.Identity,
                                     bias=bias[:]).then_inc(proj_ready, 1)

            def batch(b):
                keep_turned(b, 0)
                for q in range(1, QT):
                    keep_turned(b, q)
                    keep_product(b, q - 1)
                keep_product(b, QT - 1)
                act.drain()
                nc.scalar.copy(proj[0:PROJ, L - 1:L], b48[:]).then_inc(last_set, 1)
                act.wait_ge(last_set, b + 1)
                act.dma_start(k.proj[b, 0], proj[0:PROJ, 0:L]).then_inc(proj_stored, 16)
                act.dma_start(k.proj[b, 1], proj[HB:HB + PROJ, 1:L + 1]).then_inc(proj_stored, 16)

            peeled(act, B, batch)


def scan_states(nc, k):
    R = B * N_STATE
    with ExitStack() as ctx:
        def sb(name, shape, dt=F32):
            return ctx.enter_context(nc.sbuf_tensor("s_" + name, shape, dt))

        def sem(name):
            return ctx.enter_context(nc.semaphore("s_" + name))

        part = sb("part", [R, 3, 2, L])
        a_log = sb("a_log", [R, 1])
        e_a = sb("e_a", [R, 1])
        is_big = sb("is_big", [R, 1])
        is_small = sb("is_small", [R, 1])
        a_safe = sb("a_safe", [R, 1])
        neg_e_a = sb("neg_e_a", [R, 1])
        scale_big = sb("scale_big", [R, 1])
        neg_small = sb("neg_small", [R, 1])
        sixth = sb("sixth", [R, 1])
        t0 = sb("t0", [R, L])
        t1 = sb("t1", [R, L])
        t2 = sb("t2", [R, L])
        t3 = sb("t3", [R, L])
        t4 = sb("t4", [R, L])
        loaded = sem("loaded")
        loaded_bc = sem("loaded_bc")
        exp_ready = sem("exp_ready")
        small_ready = sem("small_ready")
        delta_ready = sem("delta_ready")
        bc_ready = sem("bc_ready")
        act_step = sem("act_step")
        log_ready = sem("log_ready")
        softplus_ready = sem("softplus_ready")
        block = ctx.enter_context(nc.Block())

        delta, bm, cm = (part[:, j, 0, :] for j in range(3))

        @block.sync
        def _(sp):
            for b in range(B):
                sp.dma_start(a_log[N_STATE * b:N_STATE * (b + 1), :], k.A_log.unsqueeze(1)).then_inc(loaded, 16)
            for half in range(2):
                for b in range(B):
                    sp.dma_start(part[N_STATE * b:N_STATE * (b + 1), 0, half, :],
                                 k.proj[b, half, 0:N_STATE, :]).then_inc(loaded, 16)
            for j in (1, 2):
                for half in range(2):
                    for b in range(B):
                        sp.dma_start(part[N_STATE * b:N_STATE * (b + 1), j, half, :],
                                     k.proj[b, half, N_STATE * j:N_STATE * (j + 1), :]).then_inc(loaded_bc, 16)

        @block.gpsimd
        def _(pool):
            nc.gpsimd.memset(k.states[R:R + 1, :], 1.0)
            pool.wait_ge(loaded, 16 * 3 * B)
            nc.gpsimd.tensor_tensor(e_a[:], k.euler[0:R, :], a_log[:], ALU.pow).then_inc(exp_ready, 1)
            pool.wait_ge(loaded_bc, 16 * 4 * B)
            for x in (1, 2):
                nc.gpsimd.tensor_tensor(part[:, x, 0, :], part[:, x, 0, :], part[:, x, 1, :],
                                        ALU.add).then_inc(bc_ready, 1)

        @block.scalar
        def _(act):
            act.wait_ge(delta_ready, 1)
            nc.scalar.activation(t0[:], delta, ACT.Abs)
            act.drain()
            nc.scalar.activation(t1[:], t0[:], ACT.Sigmoid).then_inc(act_step, 1)
            act.drain()
            nc.scalar.activation(t2[:], t1[:], ACT.Ln).then_inc(log_ready, 1)
            act.drain()
            nc.scalar.activation(t3[:], t2[:], ACT.Sigmoid).then_inc(log_ready, 1)
            act.wait_ge(softplus_ready, 1)
            act.wait_ge(small_ready, 1)
            nc.scalar.activation(t1[:], t0[:], ACT.Sigmoid, scale=neg_e_a[:]).then_inc(act_step, 1)

        @block.vector
        def _(v):
            v.wait_ge(loaded, 16 * 3 * B)
            nc.vector.tensor_tensor(delta, delta, part[:, 0, 1, :], ALU.add).then_inc(delta_ready, 1)
            v.wait_ge(exp_ready, 1)
            nc.vector.tensor_scalar(is_big[:], e_a[:], A_EPS, None, ALU.is_ge)
            nc.vector.tensor_scalar(is_small[:], e_a[:], A_EPS, None, ALU.is_lt)
            nc.vector.tensor_scalar(neg_e_a[:], e_a[:], -1.0, None, ALU.mult).then_inc(small_ready, 1)
            nc.vector.tensor_scalar(neg_small[:], e_a[:], A_EPS, -1.0, ALU.min, ALU.mult)
            v.drain()
            nc.vector.tensor_tensor(a_safe[:], e_a[:], is_small[:], ALU.max)
            nc.vector.tensor_scalar(sixth[:], neg_small[:], 1.0 / 6.0, None, ALU.mult)
            v.drain()
            nc.vector.reciprocal(scale_big[:], a_safe[:])
            v.drain()
            nc.vector.tensor_scalar(scale_big[:], scale_big[:], is_big[:], -1.0, ALU.mult, ALU.mult)
            v.wait_ge(log_ready, 2)
            nc.vector.reciprocal(t4[:], t3[:])
            v.drain()
            nc.vector.scalar_tensor_tensor(out=t4[:], in0=t4[:], scalar=-1.0, in1=t1[:], op0=ALU.add, op1=ALU.mult)
            v.drain()
            nc.vector.scalar_tensor_tensor(out=t4[:], in0=t4[:], scalar=-1.0, in1=t2[:], op0=ALU.add, op1=ALU.add)
            v.drain()
            nc.vector.scalar_tensor_tensor(out=t0[:], in0=delta, scalar=0.0, in1=t4[:], op0=ALU.max,
                                           op1=ALU.subtract).then_inc(softplus_ready, 1)
            v.drain()
            nc.vector.tensor_scalar(t2[:], t0[:], sixth[:], 0.5, ALU.mult, ALU.add)
            v.drain()
            nc.vector.scalar_tensor_tensor(out=t2[:], in0=t2[:], scalar=neg_small[:], in1=t0[:], op0=ALU.mult,
                                           op1=ALU.mult)
            v.drain()
            nc.vector.tensor_scalar(t2[:], t2[:], 1.0, is_small[:], ALU.add, ALU.mult)
            v.wait_ge(act_step, 2)
            nc.vector.tensor_scalar(t3[:], t1[:], -1.0, 1.0, ALU.mult, ALU.add)
            v.drain()
            nc.vector.reciprocal(t3[:], t3[:])
            nc.vector.tensor_scalar(t4[:], t1[:], 2.0, -1.0, ALU.mult, ALU.add)
            v.drain()
            nc.vector.tensor_tensor(t1[:], t1[:], t3[:], ALU.mult)
            nc.vector.scalar_tensor_tensor(out=t4[:], in0=t4[:], scalar=scale_big[:], in1=t3[:], op0=ALU.mult,
                                           op1=ALU.mult)
            v.drain()
            nc.vector.tensor_tensor(t4[:], t4[:], t2[:], ALU.add)
            v.drain()
            v.wait_ge(bc_ready, 2)
            nc.vector.tensor_tensor(t4[:], t4[:], bm, ALU.mult)
            v.drain()
            nc.vector.tensor_tensor_scan(t2[:], t1[:], t4[:], 0.0, ALU.mult, ALU.add)
            v.drain()
            nc.vector.tensor_tensor(k.states[0:R, :], cm, t2[:], ALU.mult)


def token_tiles(nc, k):
    G = L // P
    R = B * N_STATE + 1
    with ExitStack() as ctx:
        def sb(name, shape, dt=F32):
            return ctx.enter_context(nc.sbuf_tensor("t_" + name, shape, dt))

        def ps(name, shape, dt=F32):
            return ctx.enter_context(nc.psum_tensor("t_" + name, shape, dt))

        def sem(name):
            return ctx.enter_context(nc.semaphore("t_" + name))

        w_gu = sb("w_gu", [P, 2, DC, F])
        w_down = sb("w_down", [P, FC, D])
        w_r = sb("w_r", [P, DC, 2, E])
        x_in = sb("x_in", [P, SUB, D])
        chs = sb("chs", [R, 2, P])
        x1 = sb("x1", [P, 2, SUB, D])
        stats = sb("stats", [P, SUB, 6])
        moments = sb("moments", [P, SUB, 2])
        var_eps = sb("var_eps", [P, SUB])
        rstd = sb("rstd", [P, SUB])
        shift = sb("shift", [P, SUB])
        xn = sb("xn", [P, 2, SUB, D])
        xT = sb("xT", [P, 2, DC, P])
        sig = sb("sig", [P, 2, F])
        silu = sb("silu", [P, 2, F])
        h = sb("h", [P, 2, F])
        hT = sb("hT", [P, 2, FC, P])
        y_out = sb("y_out", [P, SUB, D])
        scores = sb("scores", [P, 2, SUB, E])
        biased = sb("biased", [P, SUB, E])
        hi4 = sb("hi4", [P, SUB, GROUPS, 4])
        lo4 = sb("lo4", [P, SUB, GROUPS, 4])
        hi2 = sb("hi2", [P, SUB, GROUPS, 2])
        mid2 = sb("mid2", [P, SUB, GROUPS, 2])
        lo2 = sb("lo2", [P, SUB, GROUPS, 2])
        hi1 = sb("hi1", [P, SUB, GROUPS])
        mid1 = sb("mid1", [P, SUB, GROUPS])
        lo1 = sb("lo1", [P, SUB, GROUPS])
        gscore = sb("gscore", [P, SUB, GROUPS])
        gsorted = sb("gsorted", [P, SUB, GROUPS])
        g_above = sb("g_above", [P, SUB, GROUPS])
        g_tied = sb("g_tied", [P, SUB, GROUPS])
        n_above = sb("n_above", [P, SUB])
        ones8 = sb("ones8", [P, GROUPS])
        g_rank = sb("g_rank", [P, SUB, GROUPS])
        g_open = sb("g_open", [P, SUB, GROUPS])
        masked = sb("masked", [P, SUB, E])
        top = sb("top", [P, SUB, TOPK])
        struck = sb("struck", [P, SUB, E])
        chosen = sb("chosen", [P, SUB, E], BF16)
        picked = sb("picked", [P, SUB, E])
        total = sb("total", [P, SUB])
        weights = sb("weights", [P, SUB, E])
        slot = sb("slot", [P, SUB, E])
        key = sb("key", [P, SUB, E])
        key8 = sb("key8", [P, SUB, TOPK])
        slot_idx = sb("slot_idx", [P, 2, SUB, TOPK], U32)
        token_idx = sb("token_idx", [P, 2, SUB], U32)
        ps_y = ps("ps_y", [P, D])
        ps_x = ps("ps_x", [P, DC, P])
        ps_r = ps("ps_r", [P, SUB, 2 * E])
        ps_gu = [ps(f"ps_gu{i}", [P, 2, F]) for i in range(2)]
        ps_h = ps("ps_h", [P, FC, P])
        ps_o = ps("ps_o", [P, D])
        ps_rank = ps("ps_rank", [P, SUB + 1, E])

        w_loaded = sem("w_loaded")
        x_loaded = [sem(f"x_loaded{i}") for i in range(SUB)]
        chs_ready = sem("chs_ready")
        y_done = sem("y_done")
        x1_made = sem("x1_made")
        var_ready = sem("var_ready")
        rstd_ready = sem("rstd_ready")
        shift_ready = sem("shift_ready")
        normed = sem("normed")
        xn_stored = [sem(f"xn_stored{i}") for i in range(2)]
        xt_done = sem("xt_done")
        xT_ready = sem("xT_ready")
        r_done = sem("r_done")
        scored = sem("scored")
        gu_done = sem("gu_done")
        sig_ready = sem("sig_ready")
        h_made = sem("h_made")
        ht_done = sem("ht_done")
        hT_ready = sem("hT_ready")
        o_done = sem("o_done")
        out_made = sem("out_made")
        out_stored = [sem(f"out_stored{i}") for i in range(SUB)]
        chosen_ready = sem("chosen_ready")
        weights_ready = sem("weights_ready")
        weights_stored = sem("weights_stored")
        rank_done = sem("rank_done")
        rank_read = sem("rank_read")
        idx_ready = sem("idx_ready")
        scatter_begun = sem("scatter_begun")
        scattered = [sem(f"scattered{i}") for i in range(2)]
        block = ctx.enter_context(nc.Block())

        rows = k.rows[0:T, :].rearrange("(b j p) d -> b j p d", j=G, p=P)
        out = k.out[0:T, :].rearrange("(b j p) d -> b j p d", j=G, p=P)

        def walk(eng, step):
            def pair(n, first, last):
                for half in range(2):
                    g = 2 * n + half
                    behind = half if first else 2
                    ahead = 1 - half if last else 2
                    for s in range(SUB):
                        step(g, half, s, behind, ahead)
            pair(0, True, False)
            pair(1, False, False)
            with eng.Fori(2, G // 2 - 1) as n:
                pair(n, False, False)
            pair(G // 2 - 1, False, True)

        @block.sync
        def _(sp):
            for j, w in enumerate((k.ws_gate, k.ws_up)):
                sp.dma_start(w_gu[:, j, :, :], w.rearrange("(p c) f -> p c f", c=DC)).then_inc(w_loaded, 16)
            sp.dma_start(w_down[:], k.ws_down.rearrange("(p c) d -> p c d", c=FC)).then_inc(w_loaded, 16)
            for j in range(2):
                sp.dma_start(w_r[:, :, j, :], k.w_router.rearrange("(p c) e -> p c e", c=DC)).then_inc(w_loaded, 16)

            def load_x(g, s):
                sp.wait_ge(x1_made, SUB * g + s + 1)
                sp.dma_start(x_in[:, s, :], k.x_blocks[s, g]).then_inc(x_loaded[s], 16)

            def store_xn(g, half, s):
                sp.wait_ge(normed, SUB * g + s + 1)
                sp.dma_start(rows[s, g, :, 0:D], xn[:, half, s, :]).then_inc(xn_stored[half], 16)

            def store_weights(g):
                sp.wait_ge(weights_ready, g + 1)
                for s in range(SUB):
                    sp.dma_start(rows[s, g, :, D:ROW], weights[:, s, :]).then_inc(weights_stored, 16)

            def store_out(g, s):
                sp.wait_ge(out_made, SUB * g + s + 2)
                sp.dma_start(out[s, g], y_out[:, s, :]).then_inc(out_stored[s], 16)

            def step(g, half, s, behind, ahead):
                if ahead >= 2:
                    load_x(g + 2, s)
                if ahead >= 1 and s >= 2:
                    for t in (2 * s - 4, 2 * s - 3):
                        store_xn(g + 1, 1 - half, t)
                if s > 0:
                    store_out(g, s - 1)
                elif behind >= 1:
                    store_out(g - 1, SUB - 1)
                if s == 0 and behind >= 2:
                    store_weights(g - 2)

            for g in range(2):
                for s in range(SUB):
                    load_x(g, s)
            for s in range(SUB):
                store_xn(0, 0, s)
            walk(sp, step)
            store_out(G - 1, SUB - 1)
            for g in (G - 2, G - 1):
                store_weights(g)
            for s in range(SUB):
                sp.wait_ge(out_stored[s], 16 * G)
            for half in range(2):
                sp.wait_ge(xn_stored[half], 16 * SUB * G // 2)
            sp.wait_ge(weights_stored, 16 * SUB * G)

        @block.gpsimd
        def _(pool):
            def deviation(g):
                pool.wait_ge(var_ready, g + 1)
                after(pool, normed, SUB * g)
                nc.gpsimd.tensor_tensor(rstd[:], var_eps[:], k.nhalf[:], ALU.pow).then_inc(rstd_ready, 1)

            def scatter(g, half, tiles):
                pool.wait_ge(idx_ready, g + 1)
                pool.sem_inc(scatter_begun, 1)
                for s in tiles:
                    for j in range(TOPK):
                        pool.indirect_dma_start(k.slots, bass.IndirectOffsetOnAxis(slot_idx[:, half, s, j:j + 1], 0),
                                                token_idx[:, half, s:s + 1], None).then_inc(scattered[half], 16)

            def step(g, half, s, behind, ahead):
                if s == 0 and behind >= 2:
                    scatter(g - 2, half, (0, 1))
                if s == 1 and ahead >= 1:
                    deviation(g + 1)
                if s == 2 and behind >= 2:
                    scatter(g - 2, half, (2, 3))

            deviation(0)
            walk(pool, step)
            for half in range(2):
                scatter(G - 2 + half, half, range(SUB))
            for half in range(2):
                pool.wait_ge(scattered[half], 16 * SUB * TOPK * G // 2)

        @block.tensor
        def _(pe):
            pe.sem_inc(xt_done, 2 * SUB)
            pe.sem_inc(gu_done, 2)
            pe.sem_inc(ht_done, 2)
            pe.sem_inc(o_done, 2)

            def ssm_out(g, half, s):
                if s == 0:
                    pe.wait_ge(chs_ready, g + 1)
                pe.wait_ge(x1_made, SUB * g + s + SUB)
                nc.tensor.matmul(ps_y[:], chs[:, half, :], k.wout[:, s, :], start=True, stop=True).then_inc(y_done, 1)

            def turn_x(g, half, s):
                i = SUB * g + s
                pe.wait_ge(normed, i + 1)
                pe.wait_ge(xT_ready, i + 1)
                chunks = xn[:, half, s, :].rearrange("p (q c) -> p c q", c=DC)
                for c in range(DC):
                    last = nc.tensor.transpose(ps_x[:, c, :], chunks[:, c, :], k.ident[:])
                last.then_inc(xt_done, 1)

            def gate_up(g, s):
                i = SUB * g + s
                pe.wait_ge(xT_ready, i + 2)
                pe.wait_ge(h_made, i + 1)
                for c in range(DC):
                    last = nc.tensor.matmul(ps_gu[s % 2][:], xT[:, s % 2, c, :], w_gu[:, :, c, :],
                                            start=(c == 0), stop=(c == DC - 1))
                last.then_inc(gu_done, 1)

            def route(g, s):
                i = SUB * g + s
                pe.wait_ge(xT_ready, i + 2)
                pe.wait_ge(scored, i + 1)
                for c in range(DC):
                    last = nc.tensor.matmul(ps_r[:, s, :], xT[:, s % 2, c, :],
                                            w_r[:, c, :, :], start=(c == 0), stop=(c == DC - 1))
                last.then_inc(r_done, 1)

            def down(g, s):
                i = SUB * g + s
                pe.wait_ge(hT_ready, i + 2)
                pe.wait_ge(out_made, i + 1)
                for c in range(FC):
                    last = nc.tensor.matmul(ps_o[:], hT[:, s % 2, c, :], w_down[:, c, :],
                                            start=(c == 0), stop=(c == FC - 1))
                last.then_inc(o_done, 1)

            def turn_h(g, s):
                i = SUB * g + s
                pe.wait_ge(h_made, i + 3)
                pe.wait_ge(hT_ready, i + 1)
                chunks = h[:, s % 2, :].rearrange("p (q c) -> p c q", c=FC)
                for c in range(FC):
                    last = nc.tensor.transpose(ps_h[:, c, :], chunks[:, c, :], k.ident[:])
                last.then_inc(ht_done, 1)

            def rank(g):
                pe.wait_ge(chosen_ready, g + 1)
                pe.wait_ge(rank_read, g + 1)
                for s in range(SUB + 1):
                    for t in range(min(s + 1, SUB)):
                        last = nc.tensor.matmul(ps_rank[:, s, :], (k.tri if t == s else k.ones)[:], chosen[:, t, :],
                                                start=(t == 0), stop=(t == min(s, SUB - 1)))
                last.then_inc(rank_done, 1)

            def step(g, half, s, behind, ahead):
                if s < 2 and ahead >= 1:
                    for t in (2 * s, 2 * s + 1):
                        ssm_out(g + 1, 1 - half, t)
                if s < SUB - 1:
                    after_this = (g, half, s + 1)
                elif ahead >= 1:
                    after_this = (g + 1, 1 - half, 0)
                else:
                    after_this = None
                if after_this:
                    turn_x(*after_this)
                gate_up(g, s)
                if after_this:
                    route(after_this[0], after_this[2])
                if s > 0:
                    down(g, s - 1)
                elif behind >= 1:
                    down(g - 1, SUB - 1)
                turn_h(g, s)
                if s == SUB - 1 and behind >= 1:
                    rank(g - 1)

            pe.wait_ge(w_loaded, 16 * 5)
            for s in range(SUB):
                ssm_out(0, 0, s)
            turn_x(0, 0, 0)
            route(0, 0)
            walk(pe, step)
            down(G - 1, SUB - 1)
            rank(G - 1)

        @block.scalar
        def _(act):
            act.sem_inc(xT_ready, 1)
            act.sem_inc(scored, SUB)
            act.sem_inc(hT_ready, 1)

            def copy_states(g, half):
                after(act, y_done, SUB * (g - 1))
                nc.scalar.copy(chs[:, half, :], k.states[:, bass.ds(P * g, P)]).then_inc(chs_ready, 1)

            def normalize(g, half, s):
                if s == 0:
                    act.wait_ge(shift_ready, g + 1)
                    after(act, xn_stored[half], 8 * SUB * (g - half))
                act.wait_ge(xt_done, SUB * g + s + 1)
                nc.scalar.activation(xn[:, half, s, :], x1[:, half, s, :], ACT.Identity, bias=shift[:, s:s + 1],
                                     scale=rstd[:, s:s + 1]).then_inc(normed, 1)

            def keep_x(g, s):
                i = SUB * g + s
                act.wait_ge(xt_done, i + 1 + 2 * SUB)
                act.wait_ge(gu_done, i + 1)
                nc.scalar.copy(xT[:, s % 2], ps_x[:]).then_inc(xT_ready, 1)

            def sigmoid(g, s):
                i = SUB * g + s
                act.wait_ge(gu_done, i + 3)
                act.wait_ge(h_made, i + 1)
                nc.scalar.activation(sig[:, s % 2, :], ps_gu[s % 2][:, 0, :], ACT.Sigmoid).then_inc(sig_ready, 1)

            def score(g, half, s):
                i = SUB * g + s
                act.wait_ge(r_done, i + 1)
                if s == 0:
                    after(act, weights_ready, g - 1)
                nc.scalar.activation(scores[:, half, s, :], ps_r[:, s, 0:E], ACT.Sigmoid).then_inc(scored, 1)

            def keep_h(g, s):
                i = SUB * g + s
                act.wait_ge(ht_done, i + 3)
                act.wait_ge(o_done, i + 1)
                nc.scalar.copy(hT[:, s % 2], ps_h[:]).then_inc(hT_ready, 1)

            def step(g, half, s, behind, ahead):
                if s > 0:
                    keep_h(g, s - 1)
                elif behind >= 1:
                    keep_h(g - 1, SUB - 1)
                if s == 1 and ahead >= 2:
                    copy_states(g + 2, half)
                if s >= 2 and ahead >= 1:
                    for t in (2 * s - 4, 2 * s - 3):
                        normalize(g + 1, 1 - half, t)
                if s < SUB - 1:
                    keep_x(g, s + 1)
                elif ahead >= 1:
                    keep_x(g + 1, 0)
                sigmoid(g, s)
                if s < SUB - 1:
                    score(g, half, s + 1)
                elif ahead >= 1:
                    score(g + 1, 1 - half, 0)

            for g in range(2):
                copy_states(g, g)
            for s in range(SUB):
                normalize(0, 0, s)
            keep_x(0, 0)
            score(0, 0, 0)
            walk(act, step)
            keep_h(G - 1, SUB - 1)

        @block.vector
        def _(v):
            v.sem_inc(x1_made, SUB)
            v.sem_inc(h_made, 2)
            v.sem_inc(out_made, 1)
            v.sem_inc(rank_read, 1)
            nc.vector.memset(ones8[:], 1.0)

            def residual(g, half, s):
                v.wait_ge(y_done, SUB * g + s + 1)
                v.wait_ge(x_loaded[s], 16 * g + 16)
                nc.vector.tensor_tensor(x1[:, half, s, :], x_in[:, s, :], ps_y[:], ALU.add).then_inc(x1_made, 1)

            def spread(g, half, tiles):
                v.drain()
                for s in tiles:
                    nc.vector.bn_stats(stats[:, s, :], x1[:, half, s, :])

            def variance():
                v.drain()
                for s in range(SUB):
                    nc.vector.bn_aggr(moments[:, s, :], stats[:, s, :])
                v.drain()
                nc.vector.tensor_scalar(var_eps[:], moments[:, :, 1], LN_EPS, None, ALU.add).then_inc(var_ready, 1)

            def shifts(g):
                v.wait_ge(rstd_ready, g + 1)
                nc.vector.scalar_tensor_tensor(out=shift[:], in0=moments[:, :, 0], scalar=-1.0, in1=rstd[:],
                                               op0=ALU.mult, op1=ALU.mult).then_inc(shift_ready, 1)

            def hidden(g, s):
                i = SUB * g + s
                v.wait_ge(sig_ready, i + 1)
                nc.vector.tensor_tensor(silu[:, s % 2, :], sig[:, s % 2, :], ps_gu[s % 2][:, 0, :], ALU.mult)
                v.drain()
                v.wait_ge(ht_done, i + 1)
                nc.vector.tensor_tensor(h[:, s % 2, :], silu[:, s % 2, :], ps_gu[s % 2][:, 1, :],
                                        ALU.mult).then_inc(h_made, 1)

            def finish(g, half, s):
                i = SUB * g + s
                v.wait_ge(o_done, i + 3)
                after(v, out_stored[s], 16 * g)
                nc.vector.tensor_tensor(y_out[:, s, :], x1[:, half, s, :], ps_o[:], ALU.add).then_inc(out_made, 1)

            def group_scores(g, half):
                v.wait_ge(scored, SUB * (g + 1) + SUB)
                nc.vector.tensor_tensor(biased[:], scores[:, half], k.router_bias[:].unsqueeze(1).to_broadcast(
                    [P, SUB, E]), ALU.add)
                v.drain()
                b4 = biased[:].rearrange("p s (g e) -> p (s g) e", e=GSIZE)
                flat = lambda a: a[:].rearrange("p s g e -> p (s g) e")
                nc.vector.tensor_tensor(flat(hi4), b4[:, :, 0:4], b4[:, :, 4:8], ALU.max)
                nc.vector.tensor_tensor(flat(lo4), b4[:, :, 0:4], b4[:, :, 4:8], ALU.min)
                v.drain()
                nc.vector.tensor_tensor(flat(hi2), flat(hi4)[:, :, 0:2], flat(hi4)[:, :, 2:4], ALU.max)
                nc.vector.tensor_tensor(flat(mid2), flat(hi4)[:, :, 0:2], flat(hi4)[:, :, 2:4], ALU.min)
                nc.vector.tensor_tensor(flat(lo2), flat(lo4)[:, :, 0:2], flat(lo4)[:, :, 2:4], ALU.max)
                v.drain()
                nc.vector.tensor_tensor(flat(lo2), flat(lo2), flat(mid2), ALU.max)
                nc.vector.tensor_tensor(hi1[:], hi2[:, :, :, 0], hi2[:, :, :, 1], ALU.max)
                nc.vector.tensor_tensor(mid1[:], hi2[:, :, :, 0], hi2[:, :, :, 1], ALU.min)
                v.drain()
                nc.vector.tensor_tensor(lo1[:], lo2[:, :, :, 0], lo2[:, :, :, 1], ALU.max)
                v.drain()
                nc.vector.tensor_tensor(lo1[:], lo1[:], mid1[:], ALU.max)
                v.drain()
                nc.vector.tensor_tensor(gscore[:], hi1[:], lo1[:], ALU.add)

            def open_groups():
                v.drain()
                for s in range(SUB):
                    nc.vector.max(gsorted[:, s, :], gscore[:, s, :])
                v.drain()
                fourth = gsorted[:, :, TOP_GROUPS - 1:TOP_GROUPS].to_broadcast([P, SUB, GROUPS])
                nc.vector.tensor_tensor(g_above[:], gscore[:], fourth, ALU.is_gt)
                nc.vector.tensor_tensor(g_tied[:], gscore[:], fourth, ALU.is_equal)
                v.drain()
                nc.vector.tensor_reduce(n_above[:], g_above[:], AX.X, ALU.add)
                v.drain()
                for s in range(SUB):
                    nc.vector.tensor_tensor_scan(g_rank[:, s, :], ones8[:], g_tied[:, s, :], n_above[:, s:s + 1],
                                                 ALU.mult, ALU.add)
                v.drain()
                nc.vector.scalar_tensor_tensor(out=g_tied[:], in0=g_rank[:], scalar=float(TOP_GROUPS), in1=g_tied[:],
                                               op0=ALU.is_le, op1=ALU.mult)
                v.drain()
                nc.vector.tensor_tensor(g_open[:], g_above[:], g_tied[:], ALU.add)

            def choose(g):
                v.drain()
                nc.vector.tensor_tensor(
                    masked[:].rearrange("p s (g e) -> p (s g) e", e=GSIZE),
                    biased[:].rearrange("p s (g e) -> p (s g) e", e=GSIZE),
                    g_open[:].rearrange("p s g -> p (s g)").unsqueeze(2).to_broadcast([P, SUB * GROUPS, GSIZE]),
                    ALU.mult)
                v.drain()
                for s in range(SUB):
                    nc.vector.max(top[:, s, :], masked[:, s, :])
                v.drain()
                for s in range(SUB):
                    nc.vector.match_replace(struck[:, s, :], top[:, s, :], masked[:, s, :], NEG)
                v.drain()
                nc.vector.tensor_tensor(chosen[:], struck[:], masked[:], ALU.not_equal).then_inc(chosen_ready, 1)

            def weigh(g, half):
                v.drain()
                nc.vector.tensor_tensor(picked[:], scores[:, half], chosen[:], ALU.mult)
                v.drain()
                nc.vector.tensor_reduce(total[:], picked[:], AX.X, ALU.add)
                v.drain()
                nc.vector.tensor_scalar(total[:], total[:], 1e-20, None, ALU.add)
                v.drain()
                nc.vector.reciprocal(total[:], total[:])
                v.drain()
                after(v, weights_stored, 16 * SUB * g)
                nc.vector.scalar_tensor_tensor(out=weights[:], in0=picked[:], scalar=ROUTED_SCALE,
                                               in1=total[:].unsqueeze(2).to_broadcast([P, SUB, E]),
                                               op0=ALU.mult, op1=ALU.mult).then_inc(weights_ready, 1)

            def place(g, half):
                v.wait_ge(rank_done, g + 1)
                nc.vector.tensor_tensor(slot[:], ps_rank[:, 0:SUB, :],
                                        k.slot_next[:].unsqueeze(1).to_broadcast([P, SUB, E]), ALU.add)
                v.drain()
                nc.vector.tensor_tensor(key[:], slot[:], chosen[:], ALU.mult)
                nc.vector.tensor_tensor(k.slot_next[:], k.slot_next[:], ps_rank[:, SUB, :],
                                        ALU.add).then_inc(rank_read, 1)
                v.drain()
                for s in range(SUB):
                    nc.vector.max(key8[:, s, :], key[:, s, :])
                v.drain()
                after(v, scattered[half], 8 * SUB * TOPK * (g - half))
                nc.vector.tensor_copy(slot_idx[:, half], key8[:])
                nc.vector.tensor_copy(token_idx[:, half], k.token_f[:])
                v.drain()
                nc.vector.tensor_scalar(k.token_f[:], k.token_f[:], float(P), None, ALU.add).then_inc(idx_ready, 1)

            def step(g, half, s, behind, ahead):
                if s < 2 and ahead >= 1:
                    for t in (2 * s, 2 * s + 1):
                        residual(g + 1, 1 - half, t)
                    spread(g + 1, 1 - half, (2 * s, 2 * s + 1))
                if s == 1 and ahead >= 1:
                    variance()
                if s == 2 and ahead >= 1:
                    shifts(g + 1)
                if s == 0 and behind >= 2:
                    place(g - 2, half)
                hidden(g, s)
                if behind >= 1:
                    if s == 0:
                        group_scores(g - 1, 1 - half)
                    elif s == 1:
                        open_groups()
                    elif s == 2:
                        choose(g - 1)
                    else:
                        weigh(g - 1, 1 - half)
                if s > 0:
                    finish(g, half, s - 1)
                elif behind >= 1:
                    finish(g - 1, 1 - half, SUB - 1)

            for s in range(SUB):
                residual(0, 0, s)
            spread(0, 0, range(SUB))
            variance()
            shifts(0)
            walk(v, step)
            finish(G - 1, 1, SUB - 1)
            place(G - 2, 0)
            group_scores(G - 1, 1)
            open_groups()
            choose(G - 1)
            weigh(G - 1, 1)
            place(G - 1, 1)


def tile_table(nc, k):
    Q = TILES // P + 1
    with ExitStack() as ctx:
        def sb(name, shape, dt=F32):
            return ctx.enter_context(nc.sbuf_tensor("q_" + name, shape, dt))

        count = sb("count", [P, E])
        ones = sb("ones", [P, E])
        begun_i = sb("begun_i", [P, E], I32)
        tiles = sb("tiles", [P, E])
        used = sb("used", [P, E])
        upto = sb("upto", [P, E])
        last = sb("last", [P, 1])
        this = sb("this", [P, Q])
        before = sb("before", [P, Q])
        expert = sb("expert", [P, Q])
        order = sb("order", [P, Q])
        order_before = sb("order_before", [P, Q])
        first = sb("first", [P, Q])
        order_i = sb("order_i", [P, Q], I32)
        place_i = sb("place_i", [P, Q], I32)
        place = sb("place", [P, Q])
        new = sb("new", [P, Q])
        scrap = sb("scrap", [P, 4 * Q, E])
        alive = sb("alive", [P, Q])
        start = sb("start", [P, Q])
        table = sb("table", [P, Q, 2], I32)
        made = ctx.enter_context(nc.semaphore("q_made"))
        stored = ctx.enter_context(nc.semaphore("q_stored"))
        block = ctx.enter_context(nc.Block())

        @block.vector
        def _(v):
            nc.vector.memset(ones[:], 1.0)
            nc.vector.tensor_tensor(count[:], k.slot_next[:], k.slot_base[:], ALU.subtract)
            v.drain()
            nc.vector.tensor_scalar(begun_i[:], count[:], float(P - 1), None, ALU.add)
            v.drain()
            nc.vector.tensor_scalar(begun_i[:], begun_i[:], P.bit_length() - 1, None, ALU.logical_shift_right)
            v.drain()
            nc.vector.tensor_copy(tiles[:], begun_i[:])
            v.drain()
            nc.vector.tensor_scalar(used[:], tiles[:], 1.0, None, ALU.min)
            nc.vector.tensor_tensor_scan(upto[:], ones[:], tiles[:], 0.0, ALU.mult, ALU.add)
            v.drain()
            nc.vector.tensor_scalar(last[:], upto[:, E - 1:E], -1.0, None, ALU.add)
            nc.vector.tensor_scalar(before[:], k.tile_f[:], -1.0, None, ALU.add)
            v.drain()
            nc.vector.tensor_scalar(this[:], k.tile_f[:], last[:], None, ALU.min)
            nc.vector.tensor_scalar(before[:], before[:], last[:], None, ALU.min)
            nc.vector.tensor_scalar(alive[:], k.tile_f[:], last[:], None, ALU.is_le)
            v.drain()
            for q in range(Q):
                for j, (tile, what, of) in enumerate(((this, expert, ones), (this, order, used),
                                                      (before, order_before, used), (this, first, tiles))):
                    nc.vector.scalar_tensor_tensor(out=scrap[:, 4 * q + j, :], in0=upto[:], scalar=tile[:, q:q + 1],
                                                   in1=of[:], op0=ALU.is_le, op1=ALU.mult, accum_out=what[:, q:q + 1])
            v.drain()
            nc.vector.tensor_tensor(start[:], k.tile_f[:], first[:], ALU.subtract)
            nc.vector.tensor_scalar(before[:], expert[:], float(REGION), float(-E * REGION), ALU.mult, ALU.add)
            v.drain()
            nc.vector.scalar_tensor_tensor(out=start[:], in0=start[:], scalar=float(P), in1=before[:], op0=ALU.mult,
                                           op1=ALU.add)
            v.drain()
            nc.vector.tensor_tensor(start[:], start[:], alive[:], ALU.mult)
            nc.vector.tensor_copy(order_i[:], order[:])
            nc.vector.tensor_tensor(order_before[:], order_before[:], order[:], ALU.not_equal)
            nc.vector.tensor_scalar(before[:], k.tile_f[:], 0.0, None, ALU.is_equal)
            v.drain()
            nc.vector.tensor_scalar(table[:, :, 0], start[:], float(E * REGION + SLOT0), None, ALU.add)
            nc.vector.tensor_scalar(place_i[:], order_i[:], WSLOTS - 1, None, ALU.bitwise_and)
            nc.vector.tensor_tensor(new[:], order_before[:], before[:], ALU.max)
            v.drain()
            nc.vector.tensor_copy(place[:], place_i[:])
            nc.vector.scalar_tensor_tensor(out=new[:], in0=expert[:], scalar=2.0, in1=new[:], op0=ALU.mult, op1=ALU.add)
            v.drain()
            nc.vector.scalar_tensor_tensor(out=table[:, :, 1], in0=new[:], scalar=float(WSLOTS), in1=place[:],
                                           op0=ALU.mult, op1=ALU.add)
            v.drain().then_inc(made, 1)

        @block.sync
        def _(sp):
            sp.wait_ge(made, 1)
            sp.dma_start(k.table.rearrange("(q p) f -> p q f", p=P), table[:]).then_inc(stored, 16)
            sp.wait_ge(stored, 16)
            sp.dma_start(k.tiles[:], k.table.rearrange("t f -> (t f)").unsqueeze(0)).then_inc(stored, 16)
            sp.wait_ge(stored, 32)


def expert_tiles(nc, k):
    XS, YS = 8, 4
    AHEAD_IDS, AHEAD_X = 5, 3
    AHEAD_W, AHEAD_SPLIT = 4, 2
    with ExitStack() as ctx:
        def sb(name, shape, dt=F32):
            return ctx.enter_context(nc.sbuf_tensor("e_" + name, shape, dt))

        def ps(name, shape, dt=F32):
            return ctx.enter_context(nc.psum_tensor("e_" + name, shape, dt))

        def sem(name):
            return ctx.enter_context(nc.semaphore("e_" + name))

        W = 2 * DC * F + FC * D
        DOWN = 2 * DC * F
        w_raw = sb("w_raw", [P, 2, W])
        w_high = sb("w_high", [P, WSLOTS, W], F32R)
        w_low = sb("w_low", [P, WSLOTS, W], F32R)
        ids = sb("ids", [P, UNROLL], U32)
        x = sb("x", [P, XS, ROW])
        weight = sb("weight", [P, XS])
        xT_high = sb("xT_high", [P, 2, DC, P], F32R)
        xT_low = sb("xT_low", [P, 2, DC, P], F32R)
        silu = sb("silu", [P, 2, F])
        h = sb("h", [P, 2, F])
        hT_high = sb("hT_high", [P, 2, FC, P], F32R)
        hT_low = sb("hT_low", [P, 2, FC, P], F32R)
        y = sb("y", [P, YS, D])
        ps_x = [ps(f"ps_x{i}", [P, DC, P]) for i in range(2)]
        ps_gu = [ps(f"ps_gu{i}", [P, 2, F]) for i in range(2)]
        ps_h = [ps(f"ps_h{i}", [P, FC, P]) for i in range(2)]
        ps_y = [ps(f"ps_y{i}", [P, D]) for i in range(2)]

        w_loaded = [sem(f"w_loaded{i}") for i in range(4)]
        ids_loaded = [sem(f"ids_loaded{i}") for i in range(UNROLL)]
        gathered = [sem(f"gathered{i}") for i in range(XS)]
        added = sem("added")
        pool_begun = sem("pool_begun")
        sp_begun = sem("sp_begun")
        act_begun = sem("act_begun")
        dve_begun = sem("dve_begun")
        xt_done = sem("xt_done")
        PARTS = (slice(0, DOWN), slice(DOWN, W))
        w_high_ready = [sem(f"w_high_ready{part}") for part in range(2)]
        w_low_ready = sem("w_low_ready")
        xT_high_ready = sem("xT_high_ready")
        xT_low_ready = sem("xT_low_ready")
        weight_ready = sem("weight_ready")
        gu_done = sem("gu_done")
        silu_ready = sem("silu_ready")
        h_made = sem("h_made")
        ht_done = sem("ht_done")
        hT_high_ready = sem("hT_high_ready")
        hT_low_ready = sem("hT_low_ready")
        y_done = sem("y_done")
        y_made = sem("y_made")
        block = ctx.enter_context(nc.Block())

        def walk(eng, step):
            for s in range(UNROLL):
                step(s, s)
            with eng.Fori(1, TILES // UNROLL - 1) as n:
                for s in range(UNROLL):
                    step(UNROLL * n + s, s)
            for s in range(UNROLL):
                step(TILES - UNROLL + s, s)

        def exists(i):
            return not isinstance(i, int) or 0 <= i < TILES

        def entry(eng, i, field, most):
            return eng.value_load(k.tiles[0:1, bass.ds(2 * i + field, 1)], min_val=0, max_val=most)

        class Words:

            def __init__(self, eng):
                self.eng, self.held = eng, [None] * UNROLL

            def load(self, i, s):
                if exists(i):
                    word = entry(self.eng, i, 1, 2 * WSLOTS * E - 1)
                    self.held[s % UNROLL] = [self.eng.snap(word & (WSLOTS - 1)), word]

            def place(self, s):
                return self.held[s][0]

            def is_new(self, s):
                return (self.held[s][1] & WSLOTS) > 0

            def expert(self, s):
                return self.held[s][1] // (2 * WSLOTS)

        def split_weights(eng, words, s, move):
            half = eng.snap(words.place(s) & 1)
            with eng.If(words.is_new(s)):
                move(half, words.place(s))

        @block.sync
        def _(sp):
            words = Words(sp)

            def load_weights(i, s):
                words.load(i, s)
                e = sp.snap(words.expert(s), min_val=0, max_val=E - 1)
                half = sp.snap(words.place(s) & 1)
                after(sp, w_low_ready, i - 1)
                sp.sem_inc(sp_begun, 1)
                for at, w in ((0, k.we_gate), (DC * F, k.we_up), (DOWN, k.we_down)):
                    sp.dma_start(w_raw[:, bass.ds(half, 1), at:at + DC * F],
                                 w[bass.ds(e, 1)].rearrange("o (p c) f -> p o (c f)", p=P),
                                 cond=words.is_new(s)).then_inc(w_loaded[s % 4], 16)

            def load_ids(i, s):
                start = entry(sp, i, 0, E * REGION + SLOT0)
                after(sp, added, 16 * (i - UNROLL + 1))
                sp.sem_inc(sp_begun, 1)
                sp.dma_start(ids[:, s:s + 1], k.slots[bass.ds(start, P), :]).then_inc(ids_loaded[s], 16)

            def step(i, s):
                if exists(i + AHEAD_W):
                    load_weights(i + AHEAD_W, (s + AHEAD_W) % UNROLL)
                if exists(i + AHEAD_IDS):
                    load_ids(i + AHEAD_IDS, (s + AHEAD_IDS) % UNROLL)

            for i in range(AHEAD_IDS):
                load_ids(i, i)
            for i in range(AHEAD_W):
                load_weights(i, i)
            walk(sp, step)

        @block.gpsimd
        def _(pool):
            def gather(i, s):
                pool.wait_ge(ids_loaded[s], 2 * i - 2 * s + 16)
                after(pool, xt_done, i - XS + 1)
                after(pool, weight_ready, i - XS + 1)
                pool.sem_inc(pool_begun, 1)
                pool.indirect_dma_start(x[:, s % XS, :], None, k.rows, bass.IndirectOffsetOnAxis(ids[:, s:s + 1], 0)) \
                    .then_inc(gathered[s % XS], 16)

            def add(i, s):
                pool.wait_ge(y_made, i + 1)
                after(pool, added, 16 * i)
                pool.sem_inc(pool_begun, 1)
                pool.indirect_dma_start(k.out, bass.IndirectOffsetOnAxis(ids[:, s:s + 1], 0), y[:, s % YS, :], None,
                                        compute_op=ALU.add).then_inc(added, 16)

            def step(i, s):
                if exists(i + AHEAD_X):
                    gather(i + AHEAD_X, (s + AHEAD_X) % UNROLL)
                if exists(i - 2):
                    add(i - 2, (s - 2) % UNROLL)

            for i in range(AHEAD_X):
                gather(i, i)
            walk(pool, step)
            for i in (2, 1):
                add(TILES - i, UNROLL - i)
            pool.wait_ge(added, 16 * TILES)

        @block.tensor
        def _(pe):
            words = Words(pe)

            def turn_x(i, s):
                pe.wait_ge(gathered[s % XS], 16 // XS * (i - s % XS) + 16)
                after(pe, xT_low_ready, i - 1)
                chunks = x[:, s % XS, 0:D].rearrange("p (q c) -> p c q", c=DC)
                for c in range(DC):
                    last = nc.tensor.transpose(ps_x[s % 2][:, c, :], chunks[:, c, :], k.ident[:])
                last.then_inc(xt_done, 1)

            def gate_up(i, s):
                place = words.place(s)
                high, low = (w[:, bass.ds(place, 1), 0:DOWN].rearrange("p o (j c f) -> p c (o j) f", j=2, c=DC)
                             for w in (w_high, w_low))
                pe.wait_ge(w_low_ready, i + 1)
                pe.wait_ge(xT_high_ready, i + 1)
                after(pe, h_made, i - 1)
                n = 0
                for x, w in ((xT_high, high), (xT_high, low), (xT_low, high)):
                    if x is xT_low:
                        pe.wait_ge(xT_low_ready, i + 1)
                    for c in range(DC):
                        last = nc.tensor.matmul(ps_gu[s % 2][:], x[:, s % 2, c, :], w[:, c], start=(n == 0),
                                                stop=(n == 3 * DC - 1))
                        n += 1
                last.then_inc(gu_done, 1)

            def down(i, s):
                place = words.place(s)
                high, low = (w[:, bass.ds(place, 1), DOWN:W].rearrange("p o (c d) -> p c (o d)", c=FC)
                             for w in (w_high, w_low))
                pe.wait_ge(hT_high_ready, i + 1)
                after(pe, y_made, i - 1)
                n = 0
                for x, w in ((hT_high, high), (hT_high, low), (hT_low, high)):
                    if x is hT_low:
                        pe.wait_ge(hT_low_ready, i + 1)
                    for c in range(FC):
                        last = nc.tensor.matmul(ps_y[s % 2][:], x[:, s % 2, c, :], w[:, c], start=(n == 0),
                                                stop=(n == 3 * FC - 1))
                        n += 1
                last.then_inc(y_done, 1)

            def turn_h(i, s):
                pe.wait_ge(h_made, i + 1)
                after(pe, hT_low_ready, i - 1)
                chunks = h[:, s % 2, :].rearrange("p (q c) -> p c q", c=FC)
                for c in range(FC):
                    last = nc.tensor.transpose(ps_h[s % 2][:, c, :], chunks[:, c, :], k.ident[:])
                last.then_inc(ht_done, 1)

            def step(i, s):
                if s == 0:
                    words.load(i - 2, s - 2)
                    words.load(i - 1, s - 1)
                    words.load(i, s)
                if exists(i + 1):
                    turn_x(i + 1, (s + 1) % UNROLL)
                gate_up(i, s)
                if s + 1 < UNROLL:
                    words.load(i + 1, s + 1)
                if exists(i - 1):
                    turn_h(i - 1, (s - 1) % UNROLL)
                if exists(i - 2):
                    down(i - 2, (s - 2) % UNROLL)

            turn_x(0, 0)
            walk(pe, step)
            turn_h(TILES - 1, UNROLL - 1)
            for i in (2, 1):
                down(TILES - i, UNROLL - i)

        @block.scalar
        def _(act):
            words = Words(act)

            def split_high(i, s):
                words.load(i, s)
                act.wait_ge(w_loaded[s % 4], 12 * (i - s % 4) + 48)
                after(act, y_done, i - WSLOTS + 1)
                for part in range(2):
                    act.sem_inc(act_begun, 1)
                    split_weights(act, words, s, lambda half, place: nc.scalar.copy(
                        w_high[:, bass.ds(place, 1), PARTS[part]], w_raw[:, bass.ds(half, 1), PARTS[part]]))
                    act.drain().then_inc(w_high_ready[part], 1)

            def keep_x(i, s):
                e = act.snap(words.expert(s), min_val=0, max_val=E - 1)
                act.wait_ge(xt_done, i + 1)
                after(act, gu_done, i - 1)
                nc.scalar.copy(xT_high[:, s % 2], ps_x[s % 2][:]).then_inc(xT_high_ready, 1)
                after(act, y_made, i - XS + 1)
                nc.scalar.copy(weight[:, s % XS:s % XS + 1], x[:, s % XS, bass.ds(e + D, 1)]).then_inc(weight_ready, 1)

            def activate(i, s):
                act.wait_ge(gu_done, i + 1)
                after(act, h_made, i - 1)
                nc.scalar.activation(silu[:, s % 2, :], ps_gu[s % 2][:, 0, :], ACT.Silu).then_inc(silu_ready, 1)

            def keep_h(i, s):
                act.wait_ge(ht_done, i + 1)
                after(act, y_done, i - 1)
                nc.scalar.copy(hT_high[:, s % 2], ps_h[s % 2][:]).then_inc(hT_high_ready, 1)

            def step(i, s):
                if s == 0:
                    words.load(i + 1, s + 1)
                if exists(i + 1):
                    keep_x(i + 1, (s + 1) % UNROLL)
                activate(i, s)
                if exists(i - 1):
                    keep_h(i - 1, (s - 1) % UNROLL)
                if exists(i + AHEAD_SPLIT):
                    split_high(i + AHEAD_SPLIT, (s + AHEAD_SPLIT) % UNROLL)

            for i in range(AHEAD_SPLIT):
                split_high(i, i)
            keep_x(0, 0)
            walk(act, step)
            keep_h(TILES - 1, UNROLL - 1)

        @block.vector
        def _(v):
            words = Words(v)

            def split_low(i, s):
                for part in range(2):
                    v.wait_ge(w_high_ready[part], i + 1)
                    v.sem_inc(dve_begun, 1)
                    split_weights(v, words, s, lambda half, place: nc.vector.tensor_tensor(
                        w_low[:, bass.ds(place, 1), PARTS[part]], w_raw[:, bass.ds(half, 1), PARTS[part]],
                        w_high[:, bass.ds(place, 1), PARTS[part]].bitcast(F32), ALU.subtract))
                v.drain().then_inc(w_low_ready, 1)

            def keep_low(i, s):
                v.wait_ge(xT_high_ready, i + 1)
                after(v, gu_done, i - 1)
                nc.vector.tensor_tensor(xT_low[:, s % 2], ps_x[s % 2][:], xT_high[:, s % 2].bitcast(F32),
                                        ALU.subtract).then_inc(xT_low_ready, 1)

            def keep_h_low(i, s):
                v.wait_ge(hT_high_ready, i + 1)
                after(v, y_done, i - 1)
                nc.vector.tensor_tensor(hT_low[:, s % 2], ps_h[s % 2][:], hT_high[:, s % 2].bitcast(F32),
                                        ALU.subtract).then_inc(hT_low_ready, 1)

            def hidden(i, s):
                v.wait_ge(silu_ready, i + 1)
                after(v, ht_done, i - 1)
                nc.vector.tensor_tensor(h[:, s % 2, :], silu[:, s % 2, :], ps_gu[s % 2][:, 1, :],
                                        ALU.mult).then_inc(h_made, 1)

            def scale(i, s):
                v.wait_ge(y_done, i + 1)
                v.wait_ge(weight_ready, i + 1)
                after(v, added, 16 * (i - YS + 1))
                nc.vector.tensor_scalar(y[:, s % YS, :], ps_y[s % 2][:], weight[:, s % XS:s % XS + 1], None,
                                        ALU.mult).then_inc(y_made, 1)

            def step(i, s):
                words.load(i + AHEAD_SPLIT, s + AHEAD_SPLIT)
                if exists(i + 1):
                    keep_low(i + 1, (s + 1) % UNROLL)
                hidden(i, s)
                if exists(i - 1):
                    keep_h_low(i - 1, (s - 1) % UNROLL)
                if exists(i - 2):
                    scale(i - 2, (s - 2) % UNROLL)
                if exists(i + AHEAD_SPLIT):
                    split_low(i + AHEAD_SPLIT, (s + AHEAD_SPLIT) % UNROLL)

            for i in range(AHEAD_SPLIT):
                words.load(i, i)
                split_low(i, i)
            keep_low(0, 0)
            walk(v, step)
            keep_h_low(TILES - 1, UNROLL - 1)
            for i in (2, 1):
                scale(TILES - i, UNROLL - i)


def program(nc, x, conv_w, conv_b, Win, b_in, Wout, b_out, A_log, w_router, b_router,
            we_gate, we_up, we_down, ws_gate, ws_up, ws_down, out):
    with ExitStack() as ctx:
        def sb(name, shape, dt=F32):
            return ctx.enter_context(nc.sbuf_tensor(name, shape, dt))

        k = Shared()
        k.x_blocks = x.rearrange("b (j p) d -> b j p d", p=P)
        k.conv_w = conv_w
        k.conv_b = conv_b
        k.Win = Win
        k.b_in = b_in
        k.Wout = Wout
        k.b_out = b_out
        k.A_log = A_log
        k.w_router = w_router
        k.b_router = b_router
        k.we_gate = we_gate
        k.we_up = we_up
        k.we_down = we_down
        k.ws_gate = ws_gate
        k.ws_up = ws_up
        k.ws_down = ws_down
        k.out = out
        k.proj = nc.dram_tensor("ssm_proj", [B, 2, PROJ, L], F32).ap()
        k.rows = nc.dram_tensor("token_rows", [T + P, ROW], F32).ap()
        k.slots = nc.dram_tensor("slot_tokens", [SLOTS, 1], U32).ap()
        k.table = nc.dram_tensor("tile_table", [(TILES // P + 1) * P, 2], I32).ap()
        k.ident = sb("ident", [P, P])
        k.tri = sb("tri", [P, P], BF16)
        k.ones = sb("ones", [P, P], BF16)
        k.nhalf = sb("nhalf", [P, SUB])
        k.euler = sb("euler", [P, 1])
        k.slot_base_i = sb("slot_base_i", [P, E], I32)
        k.slot_base = sb("slot_base", [P, E])
        k.slot_next = sb("slot_next", [P, E])
        k.token_i = sb("token_i", [P, SUB], I32)
        k.token_f = sb("token_f", [P, SUB])
        k.tile_i = sb("tile_i", [P, TILES // P + 1], I32)
        k.tile_f = sb("tile_f", [P, TILES // P + 1])
        k.router_bias = sb("router_bias", [P, E])
        k.wout = sb("wout", [B * N_STATE + 1, B, D])
        k.states = sb("states", [B * N_STATE + 1, L])
        k.tiles = sb("tiles", [1, (TILES // P + 1) * P * 2], I32)
        constants(nc, k)
        ssm_inputs(nc, k)
        scan_states(nc, k)
        token_tiles(nc, k)
        tile_table(nc, k)
        expert_tiles(nc, k)


_INS = ["L0_attn_x", "L0_attn_conv_w", "L0_attn_conv_b", "L0_attn_Win", "L0_attn_b_in", "L0_attn_Wout", "L0_attn_b_out",
        "L0_attn_A_log", "L0_ffn_w_router", "L0_ffn_b_router", "L0_ffn_we_gate", "L0_ffn_we_up", "L0_ffn_we_down",
        "L0_ffn_ws_gate", "L0_ffn_ws_up", "L0_ffn_ws_down"]


def kernel(**inputs):
    import numpy as np
    import concourse.bacc as bacc
    from concourse.bass_utils import run_bass_kernel_spmd

    nc = bacc.Bacc("TRN2", target_bir_lowering=False, num_devices=1)
    arrays, args = {}, []
    for name in _INS:
        a = np.ascontiguousarray(inputs[name])
        arrays["in_" + name] = a
        args.append(nc.dram_tensor("in_" + name, a.shape, mybir.dt.from_np(a.dtype), kind="ExternalInput").ap())
    args.append(nc.dram_tensor("out_0", (T + P, D), F32, kind="ExternalOutput").ap())
    program(nc, *args)
    result = run_bass_kernel_spmd(nc, [arrays], core_ids=[0])
    return result.results[0]["out_0"][:T].reshape(B, L, D)
```
